# Optimizing a Trainium2 kernel written in Bass

```python
import numpy as np
import jax
import jax.numpy as jnp

def _softmax(x, axis=-1):
    return jax.nn.softmax(x, axis=axis)

def _gelu(x):
    return jax.nn.gelu(x, approximate=True)

def _silu(x):
    return jax.nn.silu(x)

def _sigmoid(x):
    return jax.nn.sigmoid(x)

def _layernorm(x, axis=-1, eps=1e-05):
    m = jnp.mean(x, axis=axis, keepdims=True)
    v = jnp.var(x, axis=axis, keepdims=True)
    return (x - m) / jnp.sqrt(v + eps)

def _scatter_add(tgt, idx, src, axis=0):
    return tgt.at[idx].add(src)

def _segment_sum(src, seg, n):
    return jax.ops.segment_sum(src, seg, n)
kernel_name = 'mk_adaln_ffn_d1_seqx_r8_55236c'

def setup_inputs(seed: int=0):
    np.random.seed(seed)
    _w = jnp.asarray

    def _rec_inputs():
        import jax
        import jax.numpy as jnp
        _rk = jax.random.key(seed)
        x = -7.109e-05 + 0.9999 * jax.random.normal(jax.random.fold_in(_rk, 1), (128, 32, 512), jnp.float32)
        _lenS = 32 - jax.random.randint(jax.random.fold_in(_rk, 7), (128,), 0, max(1, 32 // 4) + 1, jnp.int32)
        _lenS2 = 32 - jax.random.randint(jax.random.fold_in(_rk, 8), (128,), 0, max(1, 32 // 4) + 1, jnp.int32)
        itok_B_0_15 = jax.random.randint(jax.random.fold_in(_rk, 11), (128,), 0, 16, jnp.int32)
        return (x, itok_B_0_15)
    x, itok_B_0_15 = _rec_inputs()

    def _L0_cond_setup():
        import jax, jax.numpy as jnp
        import numpy as np
        B, C, T = (64, 32, 512)
        S, D = (16, 32)
        key = jax.random.key(seed)
        k1, k2, k3 = jax.random.split(key, 3)
        x = jax.random.normal(k1, (B, C, T), dtype=jnp.float32)
        condition = jax.random.randint(k2, (B,), 0, S, dtype=jnp.int64)
        bound = float(np.sqrt(6.0 / C))
        weights = jax.random.uniform(k3, (S, C, D), dtype=jnp.float32, minval=-bound, maxval=bound)
        return {'x': x, 'condition': condition, 'weights': weights}
    _L0_cond_all = _L0_cond_setup()
    _L0_cond_in = {k: v for k, v in _L0_cond_all.items() if k in ('weights',)}
    del _L0_cond_all

    def _L0_ffn_setup():
        import jax, jax.numpy as jnp
        import numpy as np
        C_CLAMP = 0.5
        EPS = 1e-06
        key = jax.random.key(seed)
        ks = jax.random.split(key, 6)
        B_, S, D, O, R, E = (4, 256, 512, 512, 16, 8)
        x = jax.random.normal(ks[0], (B_, S, D), dtype=jnp.float32)
        W = jax.random.normal(ks[1], (O, D), dtype=jnp.float32) * (1.0 / np.sqrt(D))
        b = jax.random.normal(ks[2], (O,), dtype=jnp.float32) * 0.01
        A = jax.random.normal(ks[3], (E, D, R), dtype=jnp.float32) * (1.0 / np.sqrt(D))
        Bm = jax.random.normal(ks[4], (E, R, O), dtype=jnp.float32) * (1.0 / np.sqrt(R))
        p_scores = jax.random.uniform(ks[5], (E,), dtype=jnp.float32)
        return {'x': x, 'W': W, 'b': b, 'A': A, 'B': Bm, 'p_scores': p_scores}
    _L0_ffn_all = _L0_ffn_setup()
    _L0_ffn_in = {k: v for k, v in _L0_ffn_all.items() if k in ('W', 'b', 'A', 'B', 'p_scores')}
    del _L0_ffn_all
    return {'x': x, 'itok_B_0_15': itok_B_0_15, 'L0_cond_weights': _L0_cond_in['weights'], 'L0_ffn_W': _L0_ffn_in['W'], 'L0_ffn_b': _L0_ffn_in['b'], 'L0_ffn_A': _L0_ffn_in['A'], 'L0_ffn_B': _L0_ffn_in['B'], 'L0_ffn_p_scores': _L0_ffn_in['p_scores']}

def reference(x, itok_B_0_15, L0_cond_weights, L0_ffn_W, L0_ffn_b, L0_ffn_A, L0_ffn_B, L0_ffn_p_scores):
    import jax
    import jax.numpy as jnp

    def _L0_cond_ref(x, condition, weights):
        import jax, jax.numpy as jnp
        import numpy as np
        B, C, T = (64, 32, 512)
        S, D = (16, 32)
        W = weights[condition]
        return jnp.einsum('bct,bcd->bdt', x, W)

    def _L0_ffn_ref(x, W, b, A, B, p_scores):
        import jax, jax.numpy as jnp
        import numpy as np
        C_CLAMP = 0.5
        EPS = 1e-06
        z = jnp.einsum('bsd,od->bso', x, W) + b
        u = jnp.einsum('bsd,edr->ebsr', x, A)
        m = jnp.einsum('ebsr,ero,e->bso', u, B, p_scores)
        norm_z = jnp.linalg.norm(z, axis=-1, keepdims=True)
        norm_m = jnp.linalg.norm(m, axis=-1, keepdims=True)
        gamma = jnp.minimum(C_CLAMP * norm_z / (norm_m + EPS), 1.0)
        return z + gamma * m
    x = x + _L0_ffn_ref(_L0_cond_ref(x, itok_B_0_15, L0_cond_weights), L0_ffn_W, L0_ffn_b, L0_ffn_A, L0_ffn_B, L0_ffn_p_scores)
    return x

_drawn_inputs = setup_inputs


def setup_inputs(seed=0):
    import zlib

    import numpy as np

    out = dict(_drawn_inputs(seed))
    spreads = {}
    factors = {'L0_ffn_b': 8.0}
    for name, (base, spread) in spreads.items():
        noise = np.random.default_rng([zlib.crc32(name.encode()), seed]).standard_normal(out[name].shape)
        drawn = base * np.exp(spread * noise) if base else spread * noise
        out[name] = jnp.asarray(drawn.astype(out[name].dtype))
    for name, factor in factors.items():
        out[name] = (out[name] * factor).astype(out[name].dtype)
    return out
```

```python
from contextlib import ExitStack

import concourse.bass as bass
from concourse import mybir

F32 = mybir.dt.float32
F32R = mybir.dt.float32r
I32 = mybir.dt.int32
ALU = mybir.AluOpType
ACT = mybir.ActivationFunctionType

P = 128
TILES = 2
CLAMP = 0.5
EPS = 1e-6


def adaln_ffn(nc, x, cond, cond_w, w_t, bias, a_t, b_lora, p_scores, out):
    batches, chan, feat = x.shape
    nbatch = P // chan
    rows = batches * chan
    steps = rows // (P * TILES)
    K = feat // P
    O = w_t.shape[1]
    R = a_t.shape[1]
    experts = p_scores.shape[0]
    assert O == feat and R == P and nbatch * chan == P and steps % 2 == 0 and steps >= 6

    x_rows = x.rearrange("b c t -> (b c) t")
    out_rows = out.rearrange("b c t -> (b c) t")
    mix_rows = cond_w.rearrange("s c d -> (s c) d")

    with ExitStack() as ctx:
        def sb(name, shape, dt=F32):
            return ctx.enter_context(nc.sbuf_tensor(name, shape, dt))

        def psum(name, shape):
            return ctx.enter_context(nc.psum_tensor(name, shape, F32))

        def sem(name):
            return ctx.enter_context(nc.semaphore(name))

        def slots(make, name, n, *a):
            return [make(f"{name}{i}", *a) for i in range(n)]

        w_raw = sb("w_raw", [P, K, O])
        w_hi = sb("w_hi", [P, K, O], F32R)
        w_lo = sb("w_lo", [P, K, O], F32R)
        a_raw = sb("a_raw", [P, K, R])
        a_hi = sb("a_hi", [P, K, R], F32R)
        a_lo = sb("a_lo", [P, K, R], F32R)
        b_raw = sb("b_raw", [P, O])
        b_scaled = sb("b_scaled", [P, O])
        b_hi = sb("b_hi", [P, O], F32R)
        b_lo = sb("b_lo", [P, O], F32R)
        p_col = sb("p_col", [P, 1])
        bias_all = sb("bias_all", [P, O])
        cond_row = sb("cond_row", [1, batches], I32)

        mix_raw = slots(sb, "mix_raw", 2, [P, TILES * P])
        mix_hi = sb("mix_hi", [P, TILES * P], F32R)
        mix_lo = sb("mix_lo", [P, TILES * P], F32R)
        x_raw = [slots(sb, f"x_raw{par}_", TILES, [P, feat]) for par in range(2)]
        x_hi = slots(sb, "x_hi", TILES, [P, feat], F32R)
        x_lo = slots(sb, "x_lo", TILES, [P, feat], F32R)
        ht_hi = sb("ht_hi", [P, K, TILES * P], F32R)
        ht_lo = sb("ht_lo", [P, K, TILES * P], F32R)
        ut_hi = sb("ut_hi", [P, TILES * P], F32R)
        ut_lo = sb("ut_lo", [P, TILES * P], F32R)
        z_sb = slots(sb, "z_sb", TILES, [P, O])
        resid = slots(sb, "resid", TILES, [P, O])
        out_sb = slots(sb, "out_sb", TILES, [P, O])
        z_squares = slots(sb, "z_squares", TILES, [P, O])
        m_squares = slots(sb, "m_squares", TILES, [P, O])
        sumsq = slots(sb, "sumsq", TILES, [P, 2])
        norms = slots(sb, "norms", TILES, [P, 2])
        gam = slots(sb, "gam", TILES, [P, 3])

        h_ps = slots(psum, "h_ps", TILES, [P, K, P])
        z_ps = slots(psum, "z_ps", TILES, [P, O])
        m_ps = slots(psum, "m_ps", TILES, [P, O])
        u_ps = psum("u_ps", [P, TILES * P])

        cond_in = sem("cond_in")
        w_in = slots(sem, "w_in", K)
        a_in = sem("a_in")
        b_in = sem("b_in")
        p_in = sem("p_in")
        bias_in = sem("bias_in")
        mix_in = slots(sem, "mix_in", 2)
        x_in = [slots(sem, f"x_in{par}_", TILES) for par in range(2)]
        stored = slots(sem, "stored", TILES)
        mix_zeroed = sem("mix_zeroed")
        w_hi_done = sem("w_hi_done")
        w_lo_done = sem("w_lo_done")
        a_hi_done = sem("a_hi_done")
        a_lo_done = sem("a_lo_done")
        b_scaled_done = sem("b_scaled_done")
        b_hi_done = sem("b_hi_done")
        b_lo_done = sem("b_lo_done")
        x_hi_done = slots(sem, "x_hi_done", TILES)
        x_lo_done = slots(sem, "x_lo_done", TILES)
        mix_hi_done = sem("mix_hi_done")
        mix_lo_done = sem("mix_lo_done")
        h_done = slots(sem, "h_done", TILES)
        ht_hi_done = slots(sem, "ht_hi_done", TILES)
        ht_lo_done = slots(sem, "ht_lo_done", TILES)
        z_done = slots(sem, "z_done", TILES)
        z_biased = slots(sem, "z_biased", TILES)
        z_squared = slots(sem, "z_squared", TILES)
        resid_done = slots(sem, "resid_done", TILES)
        u_done = sem("u_done")
        ut_hi_done = sem("ut_hi_done")
        ut_lo_done = sem("ut_lo_done")
        m_done = slots(sem, "m_done", TILES)
        m_squared = slots(sem, "m_squared", TILES)
        norms_done = slots(sem, "norms_done", TILES)
        gam_part = slots(sem, "gam_part", TILES)
        gam_clamped = slots(sem, "gam_clamped", TILES)
        out_done = slots(sem, "out_done", TILES)

        block = ctx.enter_context(nc.Block())

        def wait_freed(eng, freed, count):
            if not (isinstance(count, int) and count == 0):
                eng.wait_ge(freed, count)

        def pairs(eng, step):
            for par in range(2):
                step(par, 0, par, True, True)
            with eng.Fori(1, steps // 2 - 1) as pair:
                for par in range(2):
                    step(2 * pair + par, pair, par, True, True)
            last = steps // 2 - 1
            for par in range(2):
                step(2 * last + par, last, par, par == 0, False)

        @block.sync
        def _(sp):
            def load_x(s, par, j):
                sp.dma_start(x_raw[par][j][:, :], x_rows[bass.ds((s * TILES + j) * P, P), :])\
                    .then_inc(x_in[par][j], 16)

            def load_mix(s, par):
                for n in range(TILES * nbatch):
                    lo = n % nbatch * chan
                    which = sp.value_load(cond_row[0:1, bass.ds(s * TILES * nbatch + n, 1)],
                                          min_val=0, max_val=cond_w.shape[0] - 1)
                    sp.dma_start(mix_raw[par][lo:lo + chan, n * chan:(n + 1) * chan],
                                 mix_rows[bass.ds(which * chan, chan), :]).then_inc(mix_in[par], 16)

            sp.dma_start(cond_row[:, :], cond.rearrange("(a b) -> a b", a=1)).then_inc(cond_in, 16)
            for j in range(TILES):
                load_x(0, 0, j)
            sp.wait_ge(cond_in, 16)
            sp.wait_ge(mix_zeroed, 2)
            load_mix(0, 0)
            for j in range(TILES):
                load_x(1, 1, j)
            load_mix(1, 1)

            def step(s, pair, par, has_next, has_after_next):
                if has_after_next:
                    sp.wait_ge(mix_hi_done, s + 1)
                    sp.wait_ge(mix_lo_done, s + 1)
                    load_mix(s + 2, par)
                    for j in range(TILES):
                        sp.wait_ge(resid_done[j], s + 1)
                        load_x(s + 2, par, j)
                for j in range(TILES):
                    sp.wait_ge(out_done[j], s + 1)
                    sp.dma_start(out_rows[bass.ds((s * TILES + j) * P, P), :], out_sb[j][:, :])\
                        .then_inc(stored[j], 16)

            pairs(sp, step)
            for j in range(TILES):
                sp.wait_ge(stored[j], 16 * steps)

        @block.gpsimd
        def _(pool):
            for par in range(2):
                nc.gpsimd.memset(mix_raw[par][:, :], 0.0).then_inc(mix_zeroed, 1)

            def step(s, pair, par, has_next, has_after_next):
                for j in range(TILES):
                    pool.wait_ge(z_biased[j], s + 1)
                    wait_freed(pool, out_done[j], s)
                    pool.wait_ge(x_in[par][j], 16 * pair + 16)
                    nc.gpsimd.tensor_tensor(resid[j][:, :], z_sb[j][:, :], x_raw[par][j][:, :], ALU.add)\
                        .then_inc(resid_done[j], 1)

            pairs(pool, step)

        @block.scalar
        def _(act):
            nc.scalar.preload_act_table(ACT.Sqrt)
            act.dma_start(w_raw[:, 0, :], w_t[0:P, :]).then_inc(w_in[0], 16)
            act.dma_start(w_raw[:, 1, :], w_t[P:2 * P, :]).then_inc(w_in[1], 16)
            act.dma_start(a_raw[:, :, :], a_t.rearrange("(k p) r -> p k r", p=P)).then_inc(a_in, 16)
            for k in range(2, K):
                act.dma_start(w_raw[:, k, :], w_t[k * P:(k + 1) * P, :]).then_inc(w_in[k], 16)
            act.dma_start(b_raw[:, :], b_lora).then_inc(b_in, 16)
            with nc.allow_non_contiguous_dma(reason="one score for each partition, once"):
                act.dma_start(p_col[:, :], p_scores.rearrange("(e a) -> e a", a=1)
                              .unsqueeze(1).to_broadcast([experts, P // experts, 1])).then_inc(p_in, 16)
            act.dma_start(bias_all[:, :], bias.rearrange("(a o) -> a o", a=1).to_broadcast([P, O]))\
                .then_inc(bias_in, 16)

            def split_mix(par, pair):
                act.wait_ge(mix_in[par], 16 * TILES * nbatch * (pair + 1))
                nc.scalar.copy(mix_hi[:, :], mix_raw[par][:, :]).then_inc(mix_hi_done, 1)

            def split_x(j, par, pair):
                act.wait_ge(x_in[par][j], 16 * pair + 16)
                nc.scalar.copy(x_hi[j][:, :], x_raw[par][j][:, :]).then_inc(x_hi_done[j], 1)

            def split_ht(j, s):
                act.wait_ge(h_done[j], s + 1)
                nc.scalar.copy(ht_hi[:, :, j * P:(j + 1) * P], h_ps[j][:, :, :]).then_inc(ht_hi_done[j], 1)

            split_x(0, 0, 0)
            split_mix(0, 0)
            split_x(1, 0, 0)
            for k in range(K):
                act.wait_ge(w_in[k], 16)
                nc.scalar.copy(w_hi[:, k, :], w_raw[:, k, :]).then_inc(w_hi_done, 1)
                if k == 0:
                    split_ht(0, 0)
                if k == 1:
                    split_ht(1, 0)
                if k == 2:
                    act.wait_ge(a_in, 16)
                    nc.scalar.copy(a_hi[:, :, :], a_raw[:, :, :]).then_inc(a_hi_done, 1)
            act.wait_ge(b_scaled_done, 1)
            nc.scalar.copy(b_hi[:, :], b_scaled[:, :]).then_inc(b_hi_done, 1)

            def step(s, pair, par, has_next, has_after_next):
                nxt = 1 - par
                nxt_pair = pair + par
                if has_next:
                    for j in range(TILES):
                        act.wait_ge(h_done[j], s + 1)
                    split_x(0, nxt, nxt_pair)
                    split_mix(nxt, nxt_pair)
                    split_x(1, nxt, nxt_pair)

                def square_z(j):
                    act.wait_ge(z_biased[j], s + 1)
                    wait_freed(act, out_done[j], s)
                    nc.scalar.activation(z_squares[j][:, :], z_sb[j][:, :], ACT.Square,
                                         accum_out=sumsq[j][:, 0:1]).then_inc(z_squared[j], 1)

                def square_m(j):
                    act.wait_ge(m_done[j], s + 1)
                    nc.scalar.activation(m_squares[j][:, :], m_ps[j][:, :], ACT.Square,
                                         accum_out=sumsq[j][:, 1:2]).then_inc(m_squared[j], 1)

                def norms_of(j):
                    act.wait_ge(z_squared[j], s + 1)
                    act.wait_ge(m_squared[j], s + 1)
                    nc.scalar.activation(norms[j][:, :], sumsq[j][:, :], ACT.Sqrt).then_inc(norms_done[j], 1)

                square_z(0)
                act.wait_ge(u_done, s + 1)
                nc.scalar.copy(ut_hi[:, :], u_ps[:, :]).then_inc(ut_hi_done, 1)
                if has_next:
                    split_ht(0, s + 1)
                square_z(1)
                square_m(0)
                norms_of(0)
                if has_next:
                    split_ht(1, s + 1)
                square_m(1)
                norms_of(1)

            pairs(act, step)

        @block.vector
        def _(dve):
            def split_mix(s, par):
                dve.wait_ge(mix_hi_done, s + 1)
                nc.vector.tensor_tensor(mix_lo[:, :], mix_raw[par][:, :], mix_hi[:, :].bitcast(F32),
                                        ALU.subtract).then_inc(mix_lo_done, 1)

            def split_x(j, s, par):
                dve.wait_ge(x_hi_done[j], s + 1)
                nc.vector.tensor_tensor(x_lo[j][:, :], x_raw[par][j][:, :], x_hi[j][:, :].bitcast(F32),
                                        ALU.subtract).then_inc(x_lo_done[j], 1)

            def split_ht(j, s):
                dve.wait_ge(ht_hi_done[j], s + 1)
                at = slice(j * P, (j + 1) * P)
                nc.vector.tensor_tensor(ht_lo[:, :, at], h_ps[j][:, :, :], ht_hi[:, :, at].bitcast(F32),
                                        ALU.subtract).then_inc(ht_lo_done[j], 1)

            split_x(0, 0, 0)
            split_mix(0, 0)
            split_x(1, 0, 0)
            for k in range(K):
                dve.wait_ge(w_hi_done, k + 1)
                nc.vector.tensor_tensor(w_lo[:, k, :], w_raw[:, k, :], w_hi[:, k, :].bitcast(F32),
                                        ALU.subtract).then_inc(w_lo_done, 1)
                if k == 0:
                    split_ht(0, 0)
                if k == 1:
                    split_ht(1, 0)
                if k == 2:
                    dve.wait_ge(a_hi_done, 1)
                    nc.vector.tensor_tensor(a_lo[:, :, :], a_raw[:, :, :], a_hi[:, :, :].bitcast(F32),
                                            ALU.subtract).then_inc(a_lo_done, 1)
            dve.wait_ge(b_in, 16)
            dve.wait_ge(p_in, 16)
            nc.vector.tensor_scalar(b_scaled[:, :], b_raw[:, :], p_col[:, 0:1], None, ALU.mult)\
                .then_inc(b_scaled_done, 1)
            dve.wait_ge(b_hi_done, 1)
            nc.vector.tensor_tensor(b_lo[:, :], b_scaled[:, :], b_hi[:, :].bitcast(F32), ALU.subtract)\
                .then_inc(b_lo_done, 1)
            dve.wait_ge(bias_in, 16)

            def step(s, pair, par, has_next, has_after_next):
                nxt = 1 - par

                def add_bias(j):
                    dve.wait_ge(z_done[j], s + 1)
                    wait_freed(dve, z_squared[j], s)
                    wait_freed(dve, resid_done[j], s)
                    nc.vector.tensor_tensor(z_sb[j][:, :], z_ps[j][:, :], bias_all[:, :], ALU.add)\
                        .then_inc(z_biased[j], 1)

                def output(j):
                    dve.wait_ge(norms_done[j], s + 1)
                    nc.vector.tensor_scalar(gam[j][:, 0:1], norms[j][:, 1:2], EPS, None, ALU.add)\
                        .then_inc(gam_part[j], 1)
                    dve.wait_ge(gam_part[j], 3 * s + 1)
                    nc.vector.reciprocal(gam[j][:, 1:2], gam[j][:, 0:1]).then_inc(gam_part[j], 1)
                    dve.wait_ge(gam_part[j], 3 * s + 2)
                    nc.vector.scalar_tensor_tensor(out=gam[j][:, 2:3], in0=norms[j][:, 0:1], scalar=CLAMP,
                                                   in1=gam[j][:, 1:2], op0=ALU.mult, op1=ALU.mult)\
                        .then_inc(gam_part[j], 1)
                    dve.wait_ge(gam_part[j], 3 * s + 3)
                    nc.vector.tensor_scalar(gam[j][:, 0:1], gam[j][:, 2:3], 1.0, None, ALU.min)\
                        .then_inc(gam_clamped[j], 1)
                    dve.wait_ge(gam_clamped[j], s + 1)
                    dve.wait_ge(resid_done[j], s + 1)
                    wait_freed(dve, stored[j], 16 * s)
                    nc.vector.scalar_tensor_tensor(out=out_sb[j][:, :], in0=m_ps[j][:, :],
                                                   scalar=gam[j][:, 0:1], in1=resid[j][:, :],
                                                   op0=ALU.mult, op1=ALU.add).then_inc(out_done[j], 1)

                if has_next:
                    split_x(0, s + 1, nxt)
                    split_mix(s + 1, nxt)
                add_bias(0)
                dve.wait_ge(ut_hi_done, s + 1)
                nc.vector.tensor_tensor(ut_lo[:, :], u_ps[:, :], ut_hi[:, :].bitcast(F32), ALU.subtract)\
                    .then_inc(ut_lo_done, 1)
                if has_next:
                    split_ht(0, s + 1)
                    split_x(1, s + 1, nxt)
                add_bias(1)
                output(0)
                if has_next:
                    split_ht(1, s + 1)
                output(1)

            pairs(dve, step)

        @block.tensor
        def _(pe):
            def mix_channels(j, s):
                pe.wait_ge(x_hi_done[j], s + 1)
                pe.wait_ge(x_lo_done[j], s + 1)
                pe.wait_ge(mix_hi_done, s + 1)
                pe.wait_ge(mix_lo_done, s + 1)
                cols = slice(j * P, (j + 1) * P)
                for k in range(K):
                    at = slice(k * P, (k + 1) * P)
                    nc.tensor.matmul(h_ps[j][:, k, :], x_hi[j][:, at], mix_hi[:, cols], start=True, stop=False)
                    nc.tensor.matmul(h_ps[j][:, k, :], x_hi[j][:, at], mix_lo[:, cols], start=False, stop=False)
                    last = nc.tensor.matmul(h_ps[j][:, k, :], x_lo[j][:, at], mix_hi[:, cols],
                                            start=False, stop=True)
                last.then_inc(h_done[j], 1)

            for j in range(TILES):
                mix_channels(j, 0)

            def step(s, pair, par, has_next, has_after_next):
                def product_z(j):
                    pe.wait_ge(ht_hi_done[j], s + 1)
                    pe.wait_ge(ht_lo_done[j], s + 1)
                    wait_freed(pe, z_biased[j], s)
                    rows_j = slice(j * P, (j + 1) * P)
                    for k in range(K):
                        pe.wait_ge(w_lo_done, k + 1)
                        nc.tensor.matmul(z_ps[j][:, :], ht_hi[:, k, rows_j], w_hi[:, k, :],
                                         start=(k == 0), stop=False)
                        nc.tensor.matmul(z_ps[j][:, :], ht_hi[:, k, rows_j], w_lo[:, k, :],
                                         start=False, stop=False)
                        last = nc.tensor.matmul(z_ps[j][:, :], ht_lo[:, k, rows_j], w_hi[:, k, :],
                                                start=False, stop=(k == K - 1))
                    last.then_inc(z_done[j], 1)

                def product_u():
                    pe.wait_ge(ht_hi_done[1], s + 1)
                    pe.wait_ge(ht_lo_done[1], s + 1)
                    pe.wait_ge(a_lo_done, 1)
                    for k in range(K):
                        nc.tensor.matmul(u_ps[:, :], a_hi[:, k, :], ht_hi[:, k, :], start=(k == 0), stop=False)
                        nc.tensor.matmul(u_ps[:, :], a_hi[:, k, :], ht_lo[:, k, :], start=False, stop=False)
                        last = nc.tensor.matmul(u_ps[:, :], a_lo[:, k, :], ht_hi[:, k, :],
                                                start=False, stop=(k == K - 1))
                    last.then_inc(u_done, 1)

                def product_m(j):
                    pe.wait_ge(ut_hi_done, s + 1)
                    pe.wait_ge(ut_lo_done, s + 1)
                    pe.wait_ge(b_lo_done, 1)
                    wait_freed(pe, out_done[j], s)
                    rows_j = slice(j * P, (j + 1) * P)
                    nc.tensor.matmul(m_ps[j][:, :], ut_hi[:, rows_j], b_hi[:, :], start=True, stop=False)
                    nc.tensor.matmul(m_ps[j][:, :], ut_hi[:, rows_j], b_lo[:, :], start=False, stop=False)
                    nc.tensor.matmul(m_ps[j][:, :], ut_lo[:, rows_j], b_hi[:, :], start=False, stop=True)\
                        .then_inc(m_done[j], 1)

                product_z(0)
                product_u()
                if has_next:
                    mix_channels(0, s + 1)
                product_z(1)
                product_m(0)
                if has_next:
                    mix_channels(1, s + 1)
                product_m(1)

            pairs(pe, step)


def kernel(x, itok_B_0_15, L0_cond_weights, L0_ffn_W, L0_ffn_b, L0_ffn_A, L0_ffn_B, L0_ffn_p_scores):
    import numpy as np
    import concourse.bacc as bacc
    from concourse.bass_utils import run_bass_kernel_spmd

    nc = bacc.Bacc("TRN2", target_bir_lowering=False, num_devices=1)
    feat = L0_ffn_W.shape[1]
    a = np.asarray(L0_ffn_A)
    b = np.asarray(L0_ffn_B)
    arrays = {
        "x": np.ascontiguousarray(x),
        "cond": np.ascontiguousarray(itok_B_0_15),
        "cond_w": np.ascontiguousarray(L0_cond_weights),
        "w_t": np.ascontiguousarray(np.asarray(L0_ffn_W).T),
        "bias": np.ascontiguousarray(L0_ffn_b),
        "a_t": np.ascontiguousarray(a.transpose(1, 0, 2).reshape(feat, -1)),
        "b_lora": np.ascontiguousarray(b.reshape(-1, b.shape[-1])),
        "p_scores": np.ascontiguousarray(L0_ffn_p_scores),
    }
    args = [nc.dram_tensor(f"in_{n}", v.shape, mybir.dt.from_np(v.dtype), kind="ExternalInput").ap()
            for n, v in arrays.items()]
    out = nc.dram_tensor("out_0", arrays["x"].shape, F32, kind="ExternalOutput").ap()
    adaln_ffn(nc, *args, out)
    r = run_bass_kernel_spmd(nc, [{f"in_{n}": v for n, v in arrays.items()}], core_ids=[0])
    return r.results[0]["out_0"]
```

```python
from contextlib import ExitStack

import concourse.bass as bass
from concourse import mybir

F32 = mybir.dt.float32
F32R = mybir.dt.float32r
I32 = mybir.dt.int32
ALU = mybir.AluOpType
ACT = mybir.ActivationFunctionType

P = 128
TILES = 2
CLAMP = 0.5
WARM_UP = 15
EPS = 1e-6


def adaln_ffn(nc, x, cond, cond_w, w_t, bias, a_t, b_lora, p_scores, out):
    batches, chan, feat = x.shape
    nbatch = P // chan
    rows = batches * chan
    tiles = rows // P
    steps = tiles // TILES
    K = feat // P
    O = w_t.shape[1]
    R = a_t.shape[1]
    experts = p_scores.shape[0]
    assert O == feat and R == P and nbatch * chan == P and steps % 2 == 0 and steps >= 6

    x_rows = x.rearrange("b c t -> (b c) t")
    out_rows = out.rearrange("b c t -> (b c) t")
    mix_rows = cond_w.rearrange("s c d -> (s c) d")

    with ExitStack() as ctx:
        def sb(name, shape, dt=F32):
            return ctx.enter_context(nc.sbuf_tensor(name, shape, dt))

        def psum(name, shape):
            return ctx.enter_context(nc.psum_tensor(name, shape, F32))

        def sem(name):
            return ctx.enter_context(nc.semaphore(name))

        def slots(make, name, n, *a):
            return [make(f"{name}{i}", *a) for i in range(n)]

        w_raw = sb("w_raw", [P, K, O])
        w_hi = sb("w_hi", [P, K, O], F32R)
        w_lo = sb("w_lo", [P, K, O], F32R)
        a_raw = sb("a_raw", [P, K, R])
        a_hi = sb("a_hi", [P, K, R], F32R)
        a_lo = sb("a_lo", [P, K, R], F32R)
        b_raw = sb("b_raw", [P, O])
        b_scaled = sb("b_scaled", [P, O])
        b_hi = sb("b_hi", [P, O], F32R)
        b_lo = sb("b_lo", [P, O], F32R)
        p_col = sb("p_col", [P, 1])
        bias_all = sb("bias_all", [P, O])
        cond_all = sb("cond_all", [P, tiles, nbatch], I32)
        part_col = sb("part_col", [P, 1], I32)
        cond_scaled = sb("cond_scaled", [P, tiles], I32)
        mix_index = sb("mix_index", [P, tiles], I32)
        index_now = slots(sb, "index_now", TILES, [P, 1], I32)
        own_block = sb("own_block", [P, nbatch, chan])
        mix_row = slots(sb, "mix_row", TILES, [P, chan])
        mix = slots(sb, "mix", TILES, [P, nbatch, chan])
        x_sb = [slots(sb, f"x_sb{par}_", TILES, [P, feat]) for par in range(2)]
        ht_hi = sb("ht_hi", [P, K, TILES * P], F32R)
        ht_lo = sb("ht_lo", [P, K, TILES * P], F32R)
        ut_hi = sb("ut_hi", [P, TILES * P], F32R)
        ut_lo = sb("ut_lo", [P, TILES * P], F32R)
        z_sb = slots(sb, "z_sb", TILES, [P, O])
        resid = slots(sb, "resid", TILES, [P, O])
        out_sb = slots(sb, "out_sb", TILES, [P, O])
        z_squares = slots(sb, "z_squares", TILES, [P, O])
        m_squares = slots(sb, "m_squares", TILES, [P, O])
        sumsq = slots(sb, "sumsq", TILES, [P, 2])
        z_norm = slots(sb, "z_norm", TILES, [P, 1])
        m_norm = slots(sb, "m_norm", TILES, [P, 1])
        gam = slots(sb, "gam", TILES, [P, 3])
        warm = sb("warm", [P, O], mybir.dt.bfloat16)

        h_ps = slots(psum, "h_ps", TILES, [P, K, P])
        z_ps = slots(psum, "z_ps", TILES, [P, O])
        m_ps = slots(psum, "m_ps", TILES, [P, O])
        u_ps = psum("u_ps", [P, TILES * P])

        cond_in = sem("cond_in")
        w_in = slots(sem, "w_in", K)
        a_in = sem("a_in")
        b_in = sem("b_in")
        p_in = sem("p_in")
        bias_in = sem("bias_in")
        mix_row_in = slots(sem, "mix_row_in", TILES)
        x_in = [slots(sem, f"x_in{par}_", TILES) for par in range(2)]
        stored = slots(sem, "stored", TILES)
        warm_set = sem("warm_set")
        block_zeroed = sem("block_zeroed")
        block_set = sem("block_set")
        part_done = sem("part_done")
        cond_scaled_done = sem("cond_scaled_done")
        mix_index_done = sem("mix_index_done")
        w_hi_done = sem("w_hi_done")
        w_lo_done = sem("w_lo_done")
        a_hi_done = sem("a_hi_done")
        a_lo_done = sem("a_lo_done")
        b_scaled_done = sem("b_scaled_done")
        b_hi_done = sem("b_hi_done")
        b_lo_done = sem("b_lo_done")
        index_done = slots(sem, "index_done", TILES)
        mix_done = slots(sem, "mix_done", TILES)
        h_done = slots(sem, "h_done", TILES)
        ht_hi_done = slots(sem, "ht_hi_done", TILES)
        ht_lo_done = slots(sem, "ht_lo_done", TILES)
        z_done = slots(sem, "z_done", TILES)
        z_biased = slots(sem, "z_biased", TILES)
        z_squared = slots(sem, "z_squared", TILES)
        resid_done = slots(sem, "resid_done", TILES)
        u_done = sem("u_done")
        ut_hi_done = sem("ut_hi_done")
        ut_lo_done = sem("ut_lo_done")
        m_done = slots(sem, "m_done", TILES)
        m_squared = slots(sem, "m_squared", TILES)
        z_norm_done = slots(sem, "z_norm_done", TILES)
        m_norm_done = slots(sem, "m_norm_done", TILES)
        m_eps_done = slots(sem, "m_eps_done", TILES)
        m_recip_done = slots(sem, "m_recip_done", TILES)
        gam_done = slots(sem, "gam_done", TILES)
        out_done = slots(sem, "out_done", TILES)

        block = ctx.enter_context(nc.Block())

        def wait_freed(eng, freed, count):
            if not (isinstance(count, int) and count == 0):
                eng.wait_ge(freed, count)

        def pairs(eng, step):
            for par in range(2):
                step(par, 0, par, True, True)
            with eng.Fori(1, steps // 2 - 1) as pair:
                for par in range(2):
                    step(2 * pair + par, pair, par, True, True)
            last = steps // 2 - 1
            for par in range(2):
                step(2 * last + par, last, par, par == 0, False)

        @block.sync
        def _(sp):
            def load_x(s, par, j):
                sp.dma_start(x_sb[par][j][:, :], x_rows[bass.ds((s * TILES + j) * P, P), :])\
                    .then_inc(x_in[par][j], 16)

            sp.dma_start(cond_all[:, :, :].rearrange("p t n -> p (t n)"),
                         cond.rearrange("(a b) -> a b", a=1).to_broadcast([P, batches])).then_inc(cond_in, 16)
            for j in range(TILES):
                load_x(0, 0, j)
            sp.wait_ge(x_in[0][TILES - 1], 16)
            sp.dma_start(b_raw[:, :], b_lora).then_inc(b_in, 16)
            with nc.allow_non_contiguous_dma(reason="one score for each partition, once"):
                sp.dma_start(p_col[:, :], p_scores.rearrange("(e a) -> e a", a=1)
                             .unsqueeze(1).to_broadcast([experts, P // experts, 1])).then_inc(p_in, 16)
            for j in range(TILES):
                load_x(1, 1, j)

            def step(s, pair, par, has_next, has_after_next):
                if has_after_next:
                    for j in range(TILES):
                        sp.wait_ge(resid_done[j], s + 1)
                        load_x(s + 2, par, j)
                for j in range(TILES):
                    sp.wait_ge(out_done[j], s + 1)
                    sp.dma_start(out_rows[bass.ds((s * TILES + j) * P, P), :], out_sb[j][:, :])\
                        .then_inc(stored[j], 16)

            pairs(sp, step)
            for j in range(TILES):
                sp.wait_ge(stored[j], 16 * steps)

        @block.gpsimd
        def _(pool):
            nc.gpsimd.iota(part_col[:, :], pattern=[[0, 1]], base=0, channel_multiplier=1).then_inc(part_done, 1)

            def take_index(s, j):
                nc.gpsimd.tensor_copy(index_now[j][:, :], mix_index[:, bass.ds(s * TILES + j, 1)])\
                    .then_inc(index_done[j], 1)

            def gather(j, index=None):
                index = index_now[j][:, 0:1] if index is None else index
                nc.gpsimd.indirect_dma_start(
                    out=mix_row[j][:, :], out_offset=None, in_=mix_rows,
                    in_offset=bass.IndirectOffsetOnAxis(ap=index, axis=0),
                ).then_inc(mix_row_in[j], 16)

            def spread(s, j):
                pool.wait_ge(mix_row_in[j], 16 * s + 16)
                wait_freed(pool, h_done[j], s)
                nc.gpsimd.tensor_tensor(mix[j][:, :, :], own_block[:, :, :],
                                        mix_row[j][:, :].unsqueeze(1).to_broadcast([P, nbatch, chan]),
                                        ALU.mult).then_inc(mix_done[j], 1)

            pool.wait_ge(mix_index_done, 1)
            for j in range(TILES):
                gather(j, mix_index[:, j:j + 1])
            pool.wait_ge(block_set, nbatch)
            for j in range(TILES):
                spread(0, j)
                take_index(1, j)
            for j in range(TILES):
                pool.wait_ge(mix_done[j], 1)
                pool.wait_ge(index_done[j], 1)
                gather(j)

            def step(s, pair, par, has_next, has_after_next):
                for j in range(TILES):
                    if has_next:
                        spread(s + 1, j)
                    if has_after_next:
                        take_index(s + 2, j)
                if has_after_next:
                    for j in range(TILES):
                        pool.wait_ge(mix_done[j], s + 2)
                        pool.wait_ge(index_done[j], s + 2)
                for j in range(TILES):
                    pool.wait_ge(z_biased[j], s + 1)
                    wait_freed(pool, out_done[j], s)
                    pool.wait_ge(x_in[par][j], 16 * pair + 16)
                    nc.gpsimd.tensor_tensor(resid[j][:, :], z_sb[j][:, :], x_sb[par][j][:, :], ALU.add)\
                        .then_inc(resid_done[j], 1)
                    if has_after_next and j == 0:
                        for i in range(TILES):
                            gather(i)

            pairs(pool, step)

        @block.scalar
        def _(act):
            nc.scalar.preload_act_table(ACT.Sqrt)
            def load_w(k):
                act.dma_start(w_raw[:, k, :], w_t[k * P:(k + 1) * P, :]).then_inc(w_in[k], 16)

            def split_w(k):
                act.wait_ge(w_in[k], 16)
                nc.scalar.copy(w_hi[:, k, :], w_raw[:, k, :]).then_inc(w_hi_done, 1)

            def split_ht(j, s):
                act.wait_ge(h_done[j], s + 1)
                nc.scalar.copy(ht_hi[:, :, j * P:(j + 1) * P], h_ps[j][:, :, :]).then_inc(ht_hi_done[j], 1)

            for k in range(K // 2):
                load_w(k)
            split_w(0)
            for k in range(K // 2, K):
                load_w(k)
            split_w(1)
            act.dma_start(a_raw[:, :, :], a_t.rearrange("(k p) r -> p k r", p=P)).then_inc(a_in, 16)
            act.dma_start(bias_all[:, :], bias.rearrange("(a o) -> a o", a=1).to_broadcast([P, O]))\
                .then_inc(bias_in, 16)
            for k in range(2, K - 1):
                split_w(k)
            split_ht(0, 0)
            split_w(K - 1)
            split_ht(1, 0)
            act.wait_ge(a_in, 16)
            nc.scalar.copy(a_hi[:, :, :], a_raw[:, :, :]).then_inc(a_hi_done, 1)
            act.wait_ge(b_scaled_done, 1)
            nc.scalar.copy(b_hi[:, :], b_scaled[:, :]).then_inc(b_hi_done, 1)

            def step(s, pair, par, has_next, has_after_next):
                def square_z(j):
                    act.wait_ge(z_biased[j], s + 1)
                    wait_freed(act, out_done[j], s)
                    nc.scalar.activation(z_squares[j][:, :], z_sb[j][:, :], ACT.Square,
                                         accum_out=sumsq[j][:, 0:1]).then_inc(z_squared[j], 1)

                def square_m(j):
                    act.wait_ge(m_done[j], s + 1)
                    nc.scalar.activation(m_squares[j][:, :], m_ps[j][:, :], ACT.Square,
                                         accum_out=sumsq[j][:, 1:2]).then_inc(m_squared[j], 1)

                def norm_z(j):
                    act.wait_ge(z_squared[j], s + 1)
                    nc.scalar.activation(z_norm[j][:, :], sumsq[j][:, 0:1], ACT.Sqrt, scale=CLAMP * CLAMP)\
                        .then_inc(z_norm_done[j], 1)

                def norm_m(j):
                    act.wait_ge(m_squared[j], s + 1)
                    nc.scalar.activation(m_norm[j][:, :], sumsq[j][:, 1:2], ACT.Sqrt)\
                        .then_inc(m_norm_done[j], 1)

                square_z(0)
                act.wait_ge(u_done, s + 1)
                nc.scalar.copy(ut_hi[:, :], u_ps[:, :]).then_inc(ut_hi_done, 1)
                norm_z(0)
                if has_next:
                    split_ht(0, s + 1)
                    square_z(1)
                    square_m(0)
                    norm_z(1)
                    norm_m(0)
                    split_ht(1, s + 1)
                    square_m(1)
                    norm_m(1)
                else:
                    for j in range(TILES):
                        square_m(j)
                        norm_m(j)
                    square_z(1)
                    norm_z(1)

            pairs(act, step)

        @block.vector
        def _(dve):
            def split_ht(j, s):
                dve.wait_ge(ht_hi_done[j], s + 1)
                at = slice(j * P, (j + 1) * P)
                nc.vector.tensor_tensor(ht_lo[:, :, at], h_ps[j][:, :, :], ht_hi[:, :, at].bitcast(F32),
                                        ALU.subtract).then_inc(ht_lo_done[j], 1)

            blocks = [slice(n * chan, (n + 1) * chan) for n in range(nbatch)]
            nc.vector.memset(warm[:, :], 0.0).then_inc(warm_set, 1)
            nc.vector.memset(own_block[:, :, :], 0.0).then_inc(block_zeroed, 1)
            dve.wait_ge(block_zeroed, 1)
            for n, at in enumerate(blocks):
                nc.vector.memset(own_block[at, n, :], 1.0).then_inc(block_set, 1)
            dve.wait_ge(cond_in, 16)
            for n, at in enumerate(blocks):
                nc.vector.tensor_scalar(cond_scaled[at, :], cond_all[at, :, n], float(chan), float(-n * chan),
                                        ALU.mult, ALU.add).then_inc(cond_scaled_done, 1)
            dve.wait_ge(cond_scaled_done, nbatch)
            dve.wait_ge(part_done, 1)
            nc.vector.tensor_tensor(mix_index[:, :], cond_scaled[:, :],
                                    part_col[:, 0:1].to_broadcast([P, tiles]), ALU.add)\
                .then_inc(mix_index_done, 1)

            def split_w(k):
                dve.wait_ge(w_hi_done, k + 1)
                nc.vector.tensor_tensor(w_lo[:, k, :], w_raw[:, k, :], w_hi[:, k, :].bitcast(F32),
                                        ALU.subtract).then_inc(w_lo_done, 1)

            for k in range(K - 1):
                split_w(k)
            split_ht(0, 0)
            split_w(K - 1)
            split_ht(1, 0)
            dve.wait_ge(a_hi_done, 1)
            nc.vector.tensor_tensor(a_lo[:, :, :], a_raw[:, :, :], a_hi[:, :, :].bitcast(F32),
                                    ALU.subtract).then_inc(a_lo_done, 1)
            dve.wait_ge(b_in, 16)
            dve.wait_ge(p_in, 16)
            nc.vector.tensor_scalar(b_scaled[:, :], b_raw[:, :], p_col[:, 0:1], None, ALU.mult)\
                .then_inc(b_scaled_done, 1)
            dve.wait_ge(b_hi_done, 1)
            nc.vector.tensor_tensor(b_lo[:, :], b_scaled[:, :], b_hi[:, :].bitcast(F32), ALU.subtract)\
                .then_inc(b_lo_done, 1)
            dve.wait_ge(bias_in, 16)

            def step(s, pair, par, has_next, has_after_next):
                def add_bias(j):
                    dve.wait_ge(z_done[j], s + 1)
                    wait_freed(dve, z_squared[j], s)
                    wait_freed(dve, resid_done[j], s)
                    nc.vector.tensor_tensor(z_sb[j][:, :], z_ps[j][:, :], bias_all[:, :], ALU.add)\
                        .then_inc(z_biased[j], 1)

                def recip_m(j):
                    dve.wait_ge(m_norm_done[j], s + 1)
                    nc.vector.tensor_scalar(gam[j][:, 0:1], m_norm[j][:, :], EPS, None, ALU.add)\
                        .then_inc(m_eps_done[j], 1)
                    dve.wait_ge(m_eps_done[j], s + 1)
                    nc.vector.reciprocal(gam[j][:, 1:2], gam[j][:, 0:1]).then_inc(m_recip_done[j], 1)

                def output(j):
                    dve.wait_ge(z_norm_done[j], s + 1)
                    dve.wait_ge(m_recip_done[j], s + 1)
                    nc.vector.tensor_scalar(gam[j][:, 2:3], gam[j][:, 1:2], z_norm[j][:, 0:1], 1.0,
                                            ALU.mult, ALU.min).then_inc(gam_done[j], 1)
                    dve.wait_ge(gam_done[j], s + 1)
                    dve.wait_ge(resid_done[j], s + 1)
                    wait_freed(dve, stored[j], 16 * s)
                    nc.vector.scalar_tensor_tensor(out=out_sb[j][:, :], in0=m_ps[j][:, :],
                                                   scalar=gam[j][:, 2:3], in1=resid[j][:, :],
                                                   op0=ALU.mult, op1=ALU.add).then_inc(out_done[j], 1)

                add_bias(0)
                dve.wait_ge(ut_hi_done, s + 1)
                nc.vector.tensor_tensor(ut_lo[:, :], u_ps[:, :], ut_hi[:, :].bitcast(F32), ALU.subtract)\
                    .then_inc(ut_lo_done, 1)
                if has_next:
                    split_ht(0, s + 1)
                    add_bias(1)
                    recip_m(0)
                    output(0)
                    split_ht(1, s + 1)
                    recip_m(1)
                    output(1)
                else:
                    for j in range(TILES):
                        recip_m(j)
                    add_bias(1)
                    for j in range(TILES):
                        output(j)

            pairs(dve, step)

        @block.tensor
        def _(pe):
            def mix_channels(j, s, pair, par):
                pe.wait_ge(x_in[par][j], 16 * pair + 16)
                pe.wait_ge(mix_done[j], s + 1)
                for k in range(K):
                    last = nc.tensor.matmul(h_ps[j][:, k, :], x_sb[par][j][:, k * P:(k + 1) * P],
                                            mix[j][:, :, :], start=True, stop=True)
                last.then_inc(h_done[j], 1)

            pe.wait_ge(warm_set, 1)
            with pe.Fori(0, WARM_UP):
                nc.tensor.matmul(z_ps[0][:, :], warm[:, 0:P], warm[:, :], start=True, stop=True)
            for j in range(TILES):
                mix_channels(j, 0, 0, 0)

            def step(s, pair, par, has_next, has_after_next):
                def product_z(j, chunks=range(K)):
                    if chunks[0] == 0:
                        pe.wait_ge(ht_hi_done[j], s + 1)
                        pe.wait_ge(ht_lo_done[j], s + 1)
                        wait_freed(pe, z_biased[j], s)
                    rows_j = slice(j * P, (j + 1) * P)
                    for k in chunks:
                        pe.wait_ge(w_lo_done, k + 1)
                        nc.tensor.matmul(z_ps[j][:, :], ht_hi[:, k, rows_j], w_hi[:, k, :],
                                         start=(k == 0), stop=False)
                        nc.tensor.matmul(z_ps[j][:, :], ht_hi[:, k, rows_j], w_lo[:, k, :],
                                         start=False, stop=False)
                        last = nc.tensor.matmul(z_ps[j][:, :], ht_lo[:, k, rows_j], w_hi[:, k, :],
                                                start=False, stop=(k == K - 1))
                    if k == K - 1:
                        last.then_inc(z_done[j], 1)

                def product_u():
                    pe.wait_ge(ht_hi_done[1], s + 1)
                    pe.wait_ge(ht_lo_done[1], s + 1)
                    pe.wait_ge(a_lo_done, 1)
                    for k in range(K):
                        nc.tensor.matmul(u_ps[:, :], a_hi[:, k, :], ht_hi[:, k, :], start=(k == 0), stop=False)
                        nc.tensor.matmul(u_ps[:, :], a_hi[:, k, :], ht_lo[:, k, :], start=False, stop=False)
                        last = nc.tensor.matmul(u_ps[:, :], a_lo[:, k, :], ht_hi[:, k, :],
                                                start=False, stop=(k == K - 1))
                    last.then_inc(u_done, 1)

                def product_m(j):
                    pe.wait_ge(ut_hi_done, s + 1)
                    pe.wait_ge(ut_lo_done, s + 1)
                    pe.wait_ge(b_lo_done, 1)
                    wait_freed(pe, out_done[j], s)
                    rows_j = slice(j * P, (j + 1) * P)
                    nc.tensor.matmul(m_ps[j][:, :], ut_hi[:, rows_j], b_hi[:, :], start=True, stop=False)
                    nc.tensor.matmul(m_ps[j][:, :], ut_hi[:, rows_j], b_lo[:, :], start=False, stop=False)
                    nc.tensor.matmul(m_ps[j][:, :], ut_lo[:, rows_j], b_hi[:, :], start=False, stop=True)\
                        .then_inc(m_done[j], 1)

                product_z(0)
                product_u()
                if has_next:
                    mix_channels(0, s + 1, pair + par, 1 - par)
                    product_z(1)
                    product_m(0)
                    mix_channels(1, s + 1, pair + par, 1 - par)
                    product_m(1)
                else:
                    product_z(1, range(K - 1))
                    product_m(0)
                    product_m(1)
                    product_z(1, range(K - 1, K))

            pairs(pe, step)


def kernel(x, itok_B_0_15, L0_cond_weights, L0_ffn_W, L0_ffn_b, L0_ffn_A, L0_ffn_B, L0_ffn_p_scores):
    import numpy as np
    import concourse.bacc as bacc
    from concourse.bass_utils import run_bass_kernel_spmd

    nc = bacc.Bacc("TRN2", target_bir_lowering=False, num_devices=1)
    feat = L0_ffn_W.shape[1]
    a = np.asarray(L0_ffn_A)
    b = np.asarray(L0_ffn_B)
    arrays = {
        "x": np.ascontiguousarray(x),
        "cond": np.ascontiguousarray(itok_B_0_15),
        "cond_w": np.ascontiguousarray(L0_cond_weights),
        "w_t": np.ascontiguousarray(np.asarray(L0_ffn_W).T),
        "bias": np.ascontiguousarray(L0_ffn_b),
        "a_t": np.ascontiguousarray(a.transpose(1, 0, 2).reshape(feat, -1)),
        "b_lora": np.ascontiguousarray(b.reshape(-1, b.shape[-1])),
        "p_scores": np.ascontiguousarray(L0_ffn_p_scores),
    }
    args = [nc.dram_tensor(f"in_{n}", v.shape, mybir.dt.from_np(v.dtype), kind="ExternalInput").ap()
            for n, v in arrays.items()]
    out = nc.dram_tensor("out_0", arrays["x"].shape, F32, kind="ExternalOutput").ap()
    adaln_ffn(nc, *args, out)
    r = run_bass_kernel_spmd(nc, [{f"in_{n}": v for n, v in arrays.items()}], core_ids=[0])
    return r.results[0]["out_0"]
```
